# Optimizing a Trainium2 kernel written in Bass

```python
import numpy as np
import jax
import jax.numpy as jnp

def _softmax(x, axis=-1):
    return jax.nn.softmax(x, axis=axis)

def _gelu(x):
    return jax.nn.gelu(x, approximate=True)

def _silu(x):
    return jax.nn.silu(x)

def _sigmoid(x):
    return jax.nn.sigmoid(x)

def _layernorm(x, axis=-1, eps=1e-05):
    m = jnp.mean(x, axis=axis, keepdims=True)
    v = jnp.var(x, axis=axis, keepdims=True)
    return (x - m) / jnp.sqrt(v + eps)

def _scatter_add(tgt, idx, src, axis=0):
    return tgt.at[idx].add(src)

def _segment_sum(src, seg, n):
    return jax.ops.segment_sum(src, seg, n)
kernel_name = 'mk_gnn_resnorm_d4_gnn_r32_ca2c45'

def setup_inputs(seed: int=0):
    np.random.seed(seed)
    _w = jnp.asarray

    def _rec_inputs():
        import jax
        import jax.numpy as jnp
        _gk = jax.random.key(seed)
        x = -0.0003713 + 1 * jax.random.normal(jax.random.fold_in(_gk, 1), (3125, 128), jnp.float32)
        src = jax.random.randint(jax.random.fold_in(_gk, 2), (50000,), 0, 3125, jnp.int32)
        dst = jnp.minimum((3125 * jax.random.uniform(jax.random.fold_in(_gk, 3), (50000,)) ** 2.0).astype(jnp.int32), 99999)
        _o = jnp.argsort(dst, stable=True)
        src = src[_o]
        dst = dst[_o]
        edge_attr_3 = 0.000844983 + 0.999762 * jax.random.normal(jax.random.fold_in(_gk, 11), (50000, 3), jnp.float32)
        edge_weight1 = jax.random.uniform(jax.random.fold_in(_gk, 13), (50000, 1), jnp.float32, 0.0, 5.99999)
        return (x, src, dst, edge_attr_3, edge_weight1)
    x, src, dst, edge_attr_3, edge_weight1 = _rec_inputs()

    def _L0_gnn_setup():
        import jax, jax.numpy as jnp
        import numpy as np
        N_NODES = 3125
        N_EDGES = 18750
        D = 128
        EPS = 1e-05

        def _linear_params(key, d_in, d_out):
            kw, kb = jax.random.split(key)
            bound = 1.0 / np.sqrt(d_in)
            w = jax.random.uniform(kw, (d_in, d_out), minval=-bound, maxval=bound, dtype=jnp.float32)
            b = jax.random.uniform(kb, (d_out,), minval=-bound, maxval=bound, dtype=jnp.float32)
            return (w, b)

        def _layernorm(h, gamma, beta):
            mu = jnp.mean(h, axis=-1, keepdims=True)
            var = jnp.mean(jnp.square(h - mu), axis=-1, keepdims=True)
            return (h - mu) * jax.lax.rsqrt(var + EPS) * gamma + beta
        key = jax.random.key(seed)
        ks = jax.random.split(key, 6)
        x = jax.random.normal(ks[0], (N_NODES, D), dtype=jnp.float32)
        edge_index = jax.random.randint(ks[1], (2, N_EDGES), 0, N_NODES, dtype=jnp.int32)
        w_m1, b_m1 = _linear_params(ks[2], 2 * D, D)
        w_m2, b_m2 = _linear_params(ks[3], D, D)
        w_u1, b_u1 = _linear_params(ks[4], 2 * D, D)
        w_u2, b_u2 = _linear_params(ks[5], D, D)
        gamma = jnp.ones((D,), dtype=jnp.float32)
        beta = jnp.zeros((D,), dtype=jnp.float32)
        return {'x': x, 'edge_index': edge_index, 'w_m1': w_m1, 'b_m1': b_m1, 'w_m2': w_m2, 'b_m2': b_m2, 'w_u1': w_u1, 'b_u1': b_u1, 'w_u2': w_u2, 'b_u2': b_u2, 'gamma': gamma, 'beta': beta}
    _L0_gnn_all = _L0_gnn_setup()
    _L0_gnn_in = {k: v for k, v in _L0_gnn_all.items() if k in ('w_m1', 'b_m1', 'w_m2', 'b_m2', 'w_u1', 'b_u1', 'w_u2', 'b_u2', 'gamma', 'beta')}
    del _L0_gnn_all

    def _L1_gnn_setup():
        import jax, jax.numpy as jnp
        import numpy as np
        NUM_LAYERS = 4
        HIDDEN = 128
        N_NODES = 50000
        N_EDGES = 25000

        def _gru_cell(inp, h, w_ih, w_hh, b_ih, b_hh):
            gi = inp @ w_ih.T + b_ih
            gh = h @ w_hh.T + b_hh
            i_r, i_z, i_n = jnp.split(gi, 3, axis=-1)
            h_r, h_z, h_n = jnp.split(gh, 3, axis=-1)
            r = jax.nn.sigmoid(i_r + h_r)
            z = jax.nn.sigmoid(i_z + h_z)
            n = jnp.tanh(i_n + r * h_n)
            return (1.0 - z) * n + z * h
        key = jax.random.key(seed)
        ks = jax.random.split(key, 8)
        s = 1.0 / np.sqrt(HIDDEN)
        node_embed = jax.random.normal(ks[0], (N_NODES, HIDDEN), dtype=jnp.float32)
        edge_index = jax.random.randint(ks[1], (2, N_EDGES), 0, N_NODES, dtype=jnp.int64)
        weight = jax.random.normal(ks[2], (NUM_LAYERS, HIDDEN, HIDDEN), dtype=jnp.float32) * s
        w_ih = jax.random.normal(ks[3], (3 * HIDDEN, HIDDEN), dtype=jnp.float32) * s
        w_hh = jax.random.normal(ks[4], (3 * HIDDEN, HIDDEN), dtype=jnp.float32) * s
        b_ih = jax.random.normal(ks[5], (3 * HIDDEN,), dtype=jnp.float32) * s
        b_hh = jax.random.normal(ks[6], (3 * HIDDEN,), dtype=jnp.float32) * s
        return {'node_embed': node_embed, 'edge_index': edge_index, 'weight': weight, 'w_ih': w_ih, 'w_hh': w_hh, 'b_ih': b_ih, 'b_hh': b_hh}
    _L1_gnn_all = _L1_gnn_setup()
    _L1_gnn_in = {k: v for k, v in _L1_gnn_all.items() if k in ('weight', 'w_ih', 'w_hh', 'b_ih', 'b_hh')}
    del _L1_gnn_all

    def _L2_gnn_setup():
        import jax, jax.numpy as jnp
        import numpy as np
        N_NODES = 3125
        N_EDGES = 50000
        D_IN = 128
        D_OUT = 128
        key = jax.random.key(seed)
        k1, k2, k3, k4 = jax.random.split(key, 4)
        x = jax.random.normal(k1, (N_NODES, D_IN), dtype=jnp.float32)
        edge_index = jax.random.randint(k2, (2, N_EDGES), 0, N_NODES, dtype=jnp.int64)
        scale = 1.0 / np.sqrt(D_IN)
        W_l = jax.random.normal(k3, (D_OUT, D_IN), dtype=jnp.float32) * scale
        W_r = jax.random.normal(k4, (D_OUT, D_IN), dtype=jnp.float32) * scale
        b = jnp.zeros((D_OUT,), dtype=jnp.float32)
        return {'x': x, 'edge_index': edge_index, 'W_l': W_l, 'W_r': W_r, 'b': b}
    _L2_gnn_all = _L2_gnn_setup()
    _L2_gnn_in = {k: v for k, v in _L2_gnn_all.items() if k in ('W_l', 'W_r', 'b')}
    del _L2_gnn_all

    def _L3_gnn_setup():
        import jax, jax.numpy as jnp
        import numpy as np
        import math
        N = 1250
        E = 20000
        HID = 128
        H = 8
        HD = HID // H
        CUTOFF = 5.0
        LN_EPS = 1e-05

        def _linear_params(key, out_d, in_d):
            k1, k2 = jax.random.split(key)
            s = 1.0 / np.sqrt(in_d)
            W = jax.random.uniform(k1, (out_d, in_d), minval=-s, maxval=s, dtype=jnp.float32)
            b = jax.random.uniform(k2, (out_d,), minval=-s, maxval=s, dtype=jnp.float32)
            return (W, b)
        key = jax.random.key(seed)
        ks = jax.random.split(key, 12)
        x = jax.random.normal(ks[0], (N, HID), dtype=jnp.float32)
        edge_index = jax.random.randint(ks[1], (2, E), 0, N, dtype=jnp.int64)
        edge_vec = jax.random.normal(ks[2], (E, 3), dtype=jnp.float32)
        edge_length = jax.random.uniform(ks[3], (E, 1), dtype=jnp.float32) * 6.0
        Wq, bq = _linear_params(ks[4], HID, HID)
        Wk, bk = _linear_params(ks[5], HID, HID)
        Wv, bv = _linear_params(ks[6], HID, HID)
        We1, be1 = _linear_params(ks[7], HID, 1)
        We2, be2 = _linear_params(ks[8], H, HID)
        Wo, bo = _linear_params(ks[9], HID, HID)
        ln_g = jnp.ones((HID,), jnp.float32)
        ln_b = jnp.zeros((HID,), jnp.float32)
        return {'x': x, 'edge_vec': edge_vec, 'edge_length': edge_length, 'Wq': Wq, 'bq': bq, 'Wk': Wk, 'bk': bk, 'Wv': Wv, 'bv': bv, 'We1': We1, 'be1': be1, 'We2': We2, 'be2': be2, 'Wo': Wo, 'bo': bo, 'ln_g': ln_g, 'ln_b': ln_b, 'edge_index': edge_index}
    _L3_gnn_all = _L3_gnn_setup()
    _L3_gnn_in = {k: v for k, v in _L3_gnn_all.items() if k in ('Wq', 'bq', 'Wk', 'bk', 'Wv', 'bv', 'We1', 'be1', 'We2', 'be2', 'Wo', 'bo', 'ln_g', 'ln_b')}
    del _L3_gnn_all
    return {'x': x, 'src': src, 'dst': dst, 'edge_attr_3': edge_attr_3, 'edge_weight1': edge_weight1, 'L0_gnn_w_m1': _L0_gnn_in['w_m1'], 'L0_gnn_b_m1': _L0_gnn_in['b_m1'], 'L0_gnn_w_m2': _L0_gnn_in['w_m2'], 'L0_gnn_b_m2': _L0_gnn_in['b_m2'], 'L0_gnn_w_u1': _L0_gnn_in['w_u1'], 'L0_gnn_b_u1': _L0_gnn_in['b_u1'], 'L0_gnn_w_u2': _L0_gnn_in['w_u2'], 'L0_gnn_b_u2': _L0_gnn_in['b_u2'], 'L0_gnn_gamma': _L0_gnn_in['gamma'], 'L0_gnn_beta': _L0_gnn_in['beta'], 'L1_gnn_weight': _L1_gnn_in['weight'], 'L1_gnn_w_ih': _L1_gnn_in['w_ih'], 'L1_gnn_w_hh': _L1_gnn_in['w_hh'], 'L1_gnn_b_ih': _L1_gnn_in['b_ih'], 'L1_gnn_b_hh': _L1_gnn_in['b_hh'], 'L2_gnn_W_l': _L2_gnn_in['W_l'], 'L2_gnn_W_r': _L2_gnn_in['W_r'], 'L2_gnn_b': _L2_gnn_in['b'], 'L3_gnn_Wq': _L3_gnn_in['Wq'], 'L3_gnn_bq': _L3_gnn_in['bq'], 'L3_gnn_Wk': _L3_gnn_in['Wk'], 'L3_gnn_bk': _L3_gnn_in['bk'], 'L3_gnn_Wv': _L3_gnn_in['Wv'], 'L3_gnn_bv': _L3_gnn_in['bv'], 'L3_gnn_We1': _L3_gnn_in['We1'], 'L3_gnn_be1': _L3_gnn_in['be1'], 'L3_gnn_We2': _L3_gnn_in['We2'], 'L3_gnn_be2': _L3_gnn_in['be2'], 'L3_gnn_Wo': _L3_gnn_in['Wo'], 'L3_gnn_bo': _L3_gnn_in['bo'], 'L3_gnn_ln_g': _L3_gnn_in['ln_g'], 'L3_gnn_ln_b': _L3_gnn_in['ln_b']}

def reference(x, src, dst, edge_attr_3, edge_weight1, L0_gnn_w_m1, L0_gnn_b_m1, L0_gnn_w_m2, L0_gnn_b_m2, L0_gnn_w_u1, L0_gnn_b_u1, L0_gnn_w_u2, L0_gnn_b_u2, L0_gnn_gamma, L0_gnn_beta, L1_gnn_weight, L1_gnn_w_ih, L1_gnn_w_hh, L1_gnn_b_ih, L1_gnn_b_hh, L2_gnn_W_l, L2_gnn_W_r, L2_gnn_b, L3_gnn_Wq, L3_gnn_bq, L3_gnn_Wk, L3_gnn_bk, L3_gnn_Wv, L3_gnn_bv, L3_gnn_We1, L3_gnn_be1, L3_gnn_We2, L3_gnn_be2, L3_gnn_Wo, L3_gnn_bo, L3_gnn_ln_g, L3_gnn_ln_b):
    import jax
    import jax.numpy as jnp

    def _L0_gnn_ref(x, edge_index, w_m1, b_m1, w_m2, b_m2, w_u1, b_u1, w_u2, b_u2, gamma, beta):
        import jax, jax.numpy as jnp
        import numpy as np
        N_NODES = 3125
        N_EDGES = 18750
        D = 128
        EPS = 1e-05

        def _linear_params(key, d_in, d_out):
            kw, kb = jax.random.split(key)
            bound = 1.0 / np.sqrt(d_in)
            w = jax.random.uniform(kw, (d_in, d_out), minval=-bound, maxval=bound, dtype=jnp.float32)
            b = jax.random.uniform(kb, (d_out,), minval=-bound, maxval=bound, dtype=jnp.float32)
            return (w, b)

        def _layernorm(h, gamma, beta):
            mu = jnp.mean(h, axis=-1, keepdims=True)
            var = jnp.mean(jnp.square(h - mu), axis=-1, keepdims=True)
            return (h - mu) * jax.lax.rsqrt(var + EPS) * gamma + beta
        row, col = (edge_index[0], edge_index[1])
        m_in = jnp.concatenate([x[row], x[col]], axis=-1)
        m = jax.nn.relu(m_in @ w_m1 + b_m1) @ w_m2 + b_m2
        agg = jax.ops.segment_sum(m, col, num_segments=x.shape[0])
        u_in = jnp.concatenate([x, agg], axis=-1)
        h = jax.nn.relu(u_in @ w_u1 + b_u1) @ w_u2 + b_u2
        return _layernorm(h, gamma, beta) + x

    def _L1_gnn_ref(node_embed, edge_index, weight, w_ih, w_hh, b_ih, b_hh):
        import jax, jax.numpy as jnp
        import numpy as np
        NUM_LAYERS = 4
        HIDDEN = 128
        N_NODES = 50000
        N_EDGES = 25000

        def _gru_cell(inp, h, w_ih, w_hh, b_ih, b_hh):
            gi = inp @ w_ih.T + b_ih
            gh = h @ w_hh.T + b_hh
            i_r, i_z, i_n = jnp.split(gi, 3, axis=-1)
            h_r, h_z, h_n = jnp.split(gh, 3, axis=-1)
            r = jax.nn.sigmoid(i_r + h_r)
            z = jax.nn.sigmoid(i_z + h_z)
            n = jnp.tanh(i_n + r * h_n)
            return (1.0 - z) * n + z * h
        src = edge_index[0]
        dst = edge_index[1]
        n_nodes = node_embed.shape[0]
        x = node_embed
        for l in range(NUM_LAYERS):
            m = x @ weight[l]
            agg = jax.ops.segment_sum(m[src], dst, num_segments=n_nodes)
            x = _gru_cell(agg, x, w_ih, w_hh, b_ih, b_hh)
        return x + node_embed

    def _L2_gnn_ref(x, edge_index, W_l, W_r, b):
        import jax, jax.numpy as jnp
        import numpy as np
        N_NODES = 3125
        N_EDGES = 50000
        D_IN = 128
        D_OUT = 128
        src = edge_index[0]
        dst = edge_index[1]
        n = x.shape[0]
        agg = jax.ops.segment_sum(x[src], dst, num_segments=n)
        cnt = jax.ops.segment_sum(jnp.ones_like(src, dtype=x.dtype), dst, num_segments=n)
        mean = agg / jnp.maximum(cnt, 1.0)[:, None]
        out = jnp.einsum('nd,od->no', mean, W_l) + b + jnp.einsum('nd,od->no', x, W_r)
        return jax.nn.relu(out)

    def _L3_gnn_ref(x, edge_vec, edge_length, Wq, bq, Wk, bk, Wv, bv, We1, be1, We2, be2, Wo, bo, ln_g, ln_b, edge_index):
        import jax, jax.numpy as jnp
        import numpy as np
        import math
        N = 1250
        E = 20000
        HID = 128
        H = 8
        HD = HID // H
        CUTOFF = 5.0
        LN_EPS = 1e-05

        def _linear_params(key, out_d, in_d):
            k1, k2 = jax.random.split(key)
            s = 1.0 / np.sqrt(in_d)
            W = jax.random.uniform(k1, (out_d, in_d), minval=-s, maxval=s, dtype=jnp.float32)
            b = jax.random.uniform(k2, (out_d,), minval=-s, maxval=s, dtype=jnp.float32)
            return (W, b)
        row, col = (edge_index[0], edge_index[1])
        n = x.shape[0]
        q = (x @ Wq.T + bq).reshape(n, H, HD)
        k = (x @ Wk.T + bk).reshape(n, H, HD)
        v = (x @ Wv.T + bv).reshape(n, H, HD)
        attn = jnp.einsum('ehd,ehd->eh', q[row], k[col]) / math.sqrt(HD)
        edge_bias = jax.nn.silu(edge_length @ We1.T + be1) @ We2.T + be2
        attn = attn + edge_bias
        cut = 0.5 * (jnp.cos(edge_length * math.pi / CUTOFF) + 1.0)
        cut = cut * (edge_length < CUTOFF).astype(jnp.float32)
        attn = attn * cut
        attn_exp = jnp.exp(attn - jnp.max(attn, axis=0, keepdims=True))
        attn_sum = jax.ops.segment_sum(attn_exp, row, num_segments=n)
        attn = attn_exp / (attn_sum[row] + 1e-08)
        out = jax.ops.segment_sum(attn[:, :, None] * v[col], row, num_segments=n)
        out = out.reshape(n, HID) @ Wo.T + bo
        h = x + out
        mu = jnp.mean(h, axis=-1, keepdims=True)
        var = jnp.mean(jnp.square(h - mu), axis=-1, keepdims=True)
        return (h - mu) / jnp.sqrt(var + LN_EPS) * ln_g + ln_b
    edge_index = jnp.stack([src, dst])
    x = _layernorm(x + _L0_gnn_ref(x, edge_index, L0_gnn_w_m1, L0_gnn_b_m1, L0_gnn_w_m2, L0_gnn_b_m2, L0_gnn_w_u1, L0_gnn_b_u1, L0_gnn_w_u2, L0_gnn_b_u2, L0_gnn_gamma, L0_gnn_beta), axis=-1)
    x = _layernorm(x + _L1_gnn_ref(x, edge_index, L1_gnn_weight, L1_gnn_w_ih, L1_gnn_w_hh, L1_gnn_b_ih, L1_gnn_b_hh), axis=-1)
    x = _layernorm(x + _L2_gnn_ref(x, edge_index, L2_gnn_W_l, L2_gnn_W_r, L2_gnn_b), axis=-1)
    x = _layernorm(x + _L3_gnn_ref(x, edge_attr_3, edge_weight1, L3_gnn_Wq, L3_gnn_bq, L3_gnn_Wk, L3_gnn_bk, L3_gnn_Wv, L3_gnn_bv, L3_gnn_We1, L3_gnn_be1, L3_gnn_We2, L3_gnn_be2, L3_gnn_Wo, L3_gnn_bo, L3_gnn_ln_g, L3_gnn_ln_b, edge_index), axis=-1)
    return x

_drawn_inputs = setup_inputs


def setup_inputs(seed=0):
    import zlib

    import numpy as np

    out = dict(_drawn_inputs(seed))
    spreads = {'L0_gnn_gamma': (1.0, 0.2),
     'L0_gnn_beta': (0.0, 0.1),
     'L2_gnn_b': (0.0, 0.1),
     'L3_gnn_ln_g': (1.0, 0.2),
     'L3_gnn_ln_b': (0.0, 0.1)}
    factors = {'edge_weight1': 52.362,
     'L3_gnn_Wq': 48.609,
     'L3_gnn_bq': 191.276,
     'L3_gnn_Wk': 46.882,
     'L3_gnn_bk': 200.0,
     'L3_gnn_bv': 152.974,
     'L3_gnn_We1': 64.0,
     'L3_gnn_be1': 64.0,
     'L3_gnn_We2': 64.0,
     'L3_gnn_be2': 200.0,
     'L3_gnn_Wv': 7.008,
     'L3_gnn_Wo': 6.757}
    for name, (base, spread) in spreads.items():
        noise = np.random.default_rng([zlib.crc32(name.encode()), seed]).standard_normal(out[name].shape)
        drawn = base * np.exp(spread * noise) if base else spread * noise
        out[name] = jnp.asarray(drawn.astype(out[name].dtype))
    for name, factor in factors.items():
        out[name] = (out[name] * factor).astype(out[name].dtype)
    return out
```

```python
from contextlib import ExitStack

import numpy as np

import concourse.bass as bass
import concourse.mybir as mybir
from concourse.alu_op_type import AluOpType as ALU

F32 = mybir.dt.float32
I32 = mybir.dt.int32
U32 = mybir.dt.uint32
ACT = mybir.ActivationFunctionType
AX = mybir.AxisListType

P = 128
N = 3125
E = 50000
D = 128
HEADS, HD = 8, 16
LAYERS = 4
WINS = -(-N // P)
NPAD = WINS * P
TAIL = N - (WINS - 1) * P
EP, EJ = 125, 400
HALF = 8
TILES = -(-((E + WINS * (P - 1)) // P) // (2 * HALF)) * (2 * HALF)
ITERS = TILES // (2 * HALF)
STEPS = 2 * ITERS
SITERS = EJ // (2 * HALF)
REC = 4
PAY = D + HEADS
CHUNK = 4
CHUNKS = [(c, min(CHUNK, WINS - c)) for c in range(0, WINS, CHUNK)]
NC = len(CHUNKS)
CUTOFF = 5.0
EPS = 1e-5
ROUND = 1.5 * 2 ** 23

DENSE = ([("turn_weights", 4), ("x0T", NC), ("p_table", NC), ("q0", NC), ("H_T", NC), ("count_T", 1),
          ("agg0", NC), ("u1", NC), ("h2", NC), ("x1T", NC)]
         + [s for l in range(LAYERS) for s in ((f"y{l}", NC), (f"gru{l}", NC))]
         + [("h_back", NC), ("x2T", NC), ("sage", NC), ("x3T", NC), ("q3", NC), ("k3", NC), ("v3", NC),
            ("max_T", 1), ("max_back", 1), ("o_T", NC), ("o_out", NC)])
BASE, _n = {}, 0
for _name, _chunks in DENSE:
    BASE[_name] = _n
    _n += _chunks

SEG = ["msg"] + [f"gru{l}" for l in range(LAYERS)] + ["sage", "values"]
SPREAD = ["msg", "scores"]
GATHER = ["msg"] + [f"gru{l}" for l in range(LAYERS)] + ["sage", "scores", "values"]

VECTORS = ["L0_gnn_b_m1", "L0_gnn_b_u2", "L0_gnn_gamma", "L0_gnn_beta", "L2_gnn_b", "L3_gnn_bq", "L3_gnn_bk",
           "L3_gnn_bv", "L3_gnn_bo", "L3_gnn_ln_g", "L3_gnn_ln_b"]
SQUARES = ["L2_gnn_W_l", "L2_gnn_W_r", "L3_gnn_Wq", "L3_gnn_Wk", "L3_gnn_Wv", "L3_gnn_Wo"]


class Chain:

    def __init__(self, eng, sem):
        self.eng, self.sem, self.n, self.i, self.per, self.k = eng, sem, 0, None, 0, 0

    def value(self):
        return self.n if self.i is None else self.i * self.per + (self.n + self.k)

    def link(self, ins):
        if self.i is None:
            self.n += 1
        else:
            self.k += 1
        ins.then_inc(self.sem, 1)
        self.eng.wait_ge(self.sem, self.value())

    def enter(self, i, per):
        self.i, self.per, self.k = i, per, 0

    def leave(self, iters):
        assert self.k == self.per, (self.k, self.per)
        self.n += iters * self.per
        self.i = None


def gnn_program(nc, a, out, dbg=None, stop=None):
    ctx = ExitStack()
    with ctx:
        def sb(name, shape, dt=F32):
            return ctx.enter_context(nc.sbuf_tensor(name, shape, dt))

        def sem(name):
            return ctx.enter_context(nc.semaphore(name))

        rec_dram = {k: nc.dram_tensor(f"table_of_records_{k}", [P * TILES, REC], I32, kind="Internal").ap() for k in ("dst", "src")}
        tab = {k: nc.dram_tensor(f"tab_{k}", [NPAD, D], F32, kind="Internal").ap() for k in GATHER}
        count_dram = nc.dram_tensor("count_row", [WINS, P], F32, kind="Internal").ap()

        iota_free = sb("iota_free", [P, P])
        iota_part = sb("iota_part", [P, 1])
        ident = sb("ident", [P, P])
        before = sb("before", [P, P])
        ones = sb("ones", [P, P])
        iota_tile = sb("iota_tile", [1, TILES])
        eps_col = sb("eps_col", [P, 1])
        halfpi_col = sb("halfpi_col", [P, 1])

        score = sb("score", [P, TILES, HEADS])
        bias_e = sb("bias_e", [P, TILES, HEADS])
        score_flat = score[0:EP, :, :].rearrange("p t h -> p (t h)")
        early = [score_flat[:, n * EJ:(n + 1) * EJ] for n in range(6)]
        edge_in = {"src": early[0].bitcast(I32), "dst": early[1].bitcast(I32)}
        len_in, win_f, word, slot_hi = early[2], early[3], early[4].bitcast(I32), early[5].bitcast(I32)
        slot = {k: sb(f"slot_{k}", [EP, EJ], I32) for k in ("dst", "src")}
        rec_whole = {k: sb(f"rec_{k}", [P, EJ, REC], I32) for k in ("dst", "src")}
        rec = {k: rec_whole[k][0:EP] for k in ("dst", "src")}
        arena = [sb(f"arena{n}", [P, WINS * EJ]) for n in (0, 1)]
        used = [0, 0]

        def later(n, cols_):
            used[n] += cols_
            assert used[n] <= WINS * EJ
            return arena[n][:, used[n] - cols_:used[n]]

        hot = arena[0][0:EP, :].rearrange("p (b j) -> p b j", j=EJ)
        rank = arena[1][0:EP, :].rearrange("p (b j) -> p b j", j=EJ)
        ends = sb("ends", [EP, WINS + 1])
        cnt_p = sb("cnt_p", [EP, WINS])
        need = sb("need", [P, WINS])
        need_i = sb("need_i", [P, WINS], I32)
        incl = sb("incl", [P, WINS])
        offs = sb("offs", [P, WINS])
        tile_cmp = arena[0][0:1, :]
        tile_win_f = arena[1][0:1, 0:TILES]
        tile_win = {k: sb(f"tile_win_{k}", [1, TILES], I32) for k in ("dst", "src")}
        stage_slot = sb("stage_slot", [EP, 2, HALF], I32)
        stage_rec = sb("stage_rec", [EP, 2, HALF, REC], I32)
        slots = {k: sb(f"slots_{k}", [P, TILES, REC], I32) for k in ("dst", "src")}

        xn = sb("xn", [P, WINS, D])
        big = later(0, NPAD).rearrange("p (w d) -> p w d", d=D)
        q_win = later(0, NPAD).rearrange("p (w d) -> p w d", d=D)
        acc_flat = later(1, WINS * PAY)
        acc = acc_flat.rearrange("p (w c) -> p w c", c=PAY)
        aggT = acc_flat[:, 0:NPAD]
        aggT_w = aggT.rearrange("p (w n) -> p w n", w=WINS)
        xT = later(1, NPAD)
        uT = later(0, NPAD)
        countT = sb("countT", [WINS, P])
        count_b = later(1, NPAD)
        settled = sb("settled", [1, 1])
        stage_idx = sb("stage_idx", [P, 2, HALF], I32)
        rows = sb("rows", [P, 2, HALF, D])
        onehot = sb("onehot", [P, 2, HALF, P])
        onehotT = sb("onehotT", [P, HALF, P])
        pay = sb("pay", [P, 2, HALF, PAY])
        late = rec_whole["dst"][:, :, :].rearrange("p j r -> p (j r)").bitcast(F32)
        cut, live, tmp_t = (late[:, n * TILES:(n + 1) * TILES] for n in range(3))
        stage_len = sb("stage_len", [P, 2, HALF])
        lenT = sb("lenT", [HALF, 2, P])
        hidT = onehotT
        hmax = sb("hmax", [P, HEADS])
        hmaxT = sb("hmaxT", [HEADS, 1])
        hdiag = sb("hdiag", [HEADS, HEADS])
        hmax_b = sb("hmax_b", [P, HEADS])
        den = sb("den", [P, WINS, HEADS])
        bn = sb("bn", [P, WINS, 6])
        mv = sb("mv", [P, WINS, 2])
        std = sb("std", [P, WINS])
        gates = q_win.rearrange("p w d -> p (w d)")[:, 0:6 * CHUNK * P].rearrange("p (g s n) -> p g s n", g=3, s=2)
        g_r, g_z, g_n = (gates[:, g] for g in range(3))

        w_m1 = sb("w_m1", [P, 2, D])
        w_m2 = sb("w_m2", [P, D])
        w_u1 = sb("w_u1", [P, 2, D])
        w_u2 = sb("w_u2", [P, D])
        w_gg = sb("w_gg", [P, LAYERS, D])
        w_raw = bias_e[:, :, :].rearrange("p t h -> p (t h)")[:, 0:12 * D].rearrange("p (k d) -> p k d", d=D)
        wT = sb("wT", [P, 12, D])
        we2_raw = sb("we2_raw", [HEADS, D])
        we2T = sb("we2T", [P, HEADS])
        rowv = sb("rowv", [P, len(VECTORS), D])
        be2 = sb("be2", [P, HEADS])
        cols = sb("cols", [P, 10])
        b_rz = sb("b_rz", [P, 2])
        we1_sel = sb("we1_sel", [HALF, HALF, P])
        we1_row = sb("we1_row", [HALF, P])

        ps = ctx.enter_context(nc.psum_tensor("ps", [P, 8, 512], F32))

        def bank(b, cols_=512):
            return ps[:, b, 0:cols_]

        def eight(b):
            return ps[:, b:b + 2, :].rearrange("p b (k c) -> p (b k) c", c=P)

        def seg_slot(k, width):
            return ps[:, 4 + k // 3, (k % 3) * PAY:(k % 3) * PAY + width]

        def vec(name, n=1):
            v = rowv[:, VECTORS.index(name):VECTORS.index(name) + 1, :]
            return v.broadcast_to([P, n, D]) if n > 1 else v

        DVE, PE = mybir.EngineType.DVE, mybir.EngineType.PE

        def windows_of(engine, key, i, h):
            return nc.values_load_multi_w_load_instructions(
                tile_win[key][0:1, bass.ds(i * (2 * HALF) + h * HALF, HALF)], engines=(engine,), min_val=0, max_val=WINS - 1,
                skip_runtime_bounds_check_because="place() counts at most WINS - 1 windows before a tile")[1]

        s_iota = sem("s_iota")
        s_const = sem("s_const")
        s_edges = sem("s_edges")
        s_x = sem("s_x")
        s_w = sem("s_w")
        s_padrec = sem("s_padrec")
        s_padfill = sem("s_padfill")
        s_binned = sem("s_binned")
        s_totals = sem("s_totals")
        s_slots = sem("s_slots")
        s_scat = [sem(f"s_scat{h}") for h in (0, 1)]
        s_sorted = {k: sem(f"s_sorted_{k}") for k in ("dst", "src")}
        s_filled = sem("s_filled")
        s_emptied = sem("s_emptied")
        s_table = sem("s_table")
        s_got = [sem(f"s_got{h}") for h in (0, 1)]
        s_hot = sem("s_hot")
        s_turned = sem("s_turned")
        s_hotT = sem("s_hotT")
        s_spread = sem("s_spread")
        s_mixed = sem("s_mixed")
        s_paid = sem("s_paid")
        s_seg = sem("s_seg")
        s_added = sem("s_added")
        s_zero = sem("s_zero")
        s_norm = sem("s_norm")
        s_std = sem("s_std")
        s_gates = sem("s_gates")
        s_cand = sem("s_cand")
        s_tanh = sem("s_tanh")
        s_count = sem("s_count")
        s_stage = sem("s_stage")
        s_len = sem("s_len")
        s_lenT = sem("s_lenT")
        s_lenS = sem("s_lenS")
        s_pre = sem("s_pre")
        s_hid = sem("s_hid")
        s_eb = sem("s_eb")
        s_ebt = sem("s_ebt")
        s_cutarg = sem("s_cutarg")
        s_cut = sem("s_cut")
        s_exp = sem("s_exp")
        s_out = sem("s_out")
        s_dch = sem("s_dch")
        s_ach = sem("s_ach")
        s_pch = sem("s_pch")

        STAGE = {n: i + 1 for i, n in enumerate(
            ["consts", "x1", "x2", "means", "x3", "scored", "max_diag", "exp_arg", "out_norm", "done"])}

        N_W = 26 + len(VECTORS)

        block = ctx.enter_context(nc.Block())

        @block.sync
        def _(sp):
            for k in ("dst", "src"):
                sp.dma_start(edge_in[k][:, :], a[k].rearrange("(p j) -> p j", p=EP)).then_inc(s_edges, 16)
            sp.dma_start(len_in[:, :], a["edge_weight1"].rearrange("(p j) o -> p (j o)", p=EP)).then_inc(s_edges, 16)
            sp.wait_ge(s_zero, 1)
            sp.dma_start(xn[:, 0:WINS - 1, :], a["x"][0:(WINS - 1) * P, :].rearrange("(w p) d -> p w d", p=P)).then_inc(s_x, 16)
            sp.dma_start(xn[0:TAIL, WINS - 1, :], a["x"][(WINS - 1) * P:N, :]).then_inc(s_x, 16)
            for k in ("dst", "src"):
                sp.wait_ge(s_padfill, 1)
                sp.dma_start(rec_dram[k].rearrange("(p t) r -> p t r", p=P), slots[k][:, :, :]).then_inc(s_padrec, 16)

            def w(dst, src):
                sp.dma_start(dst, src).then_inc(s_w, 16)

            w(w_m1[:, :, :], a["L0_gnn_w_m1"].rearrange("(k p) n -> p k n", p=P))
            w(w_m2[:, :], a["L0_gnn_w_m2"])
            w(w_u1[:, :, :], a["L0_gnn_w_u1"].rearrange("(k p) n -> p k n", p=P))
            w(w_u2[:, :], a["L0_gnn_w_u2"])
            w(w_gg[:, :, :], a["L1_gnn_weight"].rearrange("l p n -> p l n"))
            w(w_raw[:, 0:3, :], a["L1_gnn_w_ih"].rearrange("(k p) n -> p k n", p=P))
            w(w_raw[:, 3:6, :], a["L1_gnn_w_hh"].rearrange("(k p) n -> p k n", p=P))
            for i, n in enumerate(SQUARES):
                w(w_raw[:, 6 + i, :], a[n])
            w(we2_raw[:, :], a["L3_gnn_We2"])
            for i, n in enumerate(VECTORS):
                w(rowv[:, i, :], a[n].unsqueeze(0).broadcast_to([P, D]))
            w(be2[:, :], a["L3_gnn_be2"].unsqueeze(0).broadcast_to([P, HEADS]))
            w(cols[:, 0:1], a["L0_gnn_b_m2"].unsqueeze(1))
            w(cols[:, 1:2], a["L0_gnn_b_u1"].unsqueeze(1))
            for k in range(3):
                w(cols[:, 2 + k:3 + k], a["L1_gnn_b_ih"][k * P:(k + 1) * P].unsqueeze(1))
                w(cols[:, 5 + k:6 + k], a["L1_gnn_b_hh"][k * P:(k + 1) * P].unsqueeze(1))
            w(cols[:, 8:9], a["L3_gnn_be1"].unsqueeze(1))
            w(cols[:, 9:10], a["L3_gnn_We1"])
            w(we1_row[:, :], a["L3_gnn_We1"].rearrange("p o -> o p").broadcast_to([HALF, P]))

            for n, k in enumerate(("dst", "src")):
                for h in (0, 1):
                    sp.wait_ge(s_scat[h], (n + 1) * SITERS * 16 * HALF)
                sp.dma_start(slots[k][:, :, :], rec_dram[k].rearrange("(p t) r -> p t r", p=P)).then_inc(s_sorted[k], 16)

            def store_table(k, stage, source):
                for c, (w0, nw) in enumerate(CHUNKS):
                    sp.wait_ge(s_emptied, BASE[stage] + c + 1)
                    sp.dma_start(tab[k][w0 * P:(w0 + nw) * P, :].rearrange("(w p) d -> p w d", p=P),
                                 source[:, w0:w0 + nw, :]).then_inc(s_table, 16)

            store_table("msg", "p_table", big)
            sp.wait_ge(s_emptied, BASE["count_T"] + 1)
            sp.dma_start(count_dram, countT[:, :]).then_inc(s_count, 16)
            sp.wait_ge(s_count, 16)
            sp.dma_start(count_b[:, :], count_dram.rearrange("w p -> (w p)").unsqueeze(0).broadcast_to([P, NPAD])).then_inc(s_count, 16)
            for l in range(LAYERS):
                store_table(f"gru{l}", f"y{l}", big)
            sp.wait_ge(s_stage, STAGE["x2"])
            for c, (w0, nw) in enumerate(CHUNKS):
                sp.dma_start(tab["sage"][w0 * P:(w0 + nw) * P, :].rearrange("(w p) d -> p w d", p=P),
                             xn[:, w0:w0 + nw, :]).then_inc(s_table, 16)
            store_table("scores", "k3", big)
            store_table("values", "v3", big)

            sp.wait_ge(s_stage, STAGE["done"])
            sp.dma_start(out[0:(WINS - 1) * P, :].rearrange("(w p) d -> p w d", p=P), xn[:, 0:WINS - 1, :]).then_inc(s_out, 16)
            sp.dma_start(out[(WINS - 1) * P:N, :], xn[0:TAIL, WINS - 1, :]).then_inc(s_out, 16)
            sp.wait_ge(s_out, 32)

        @block.gpsimd
        def _(pool):
            nc.gpsimd.iota(iota_free[:, :], [[1, P]], base=0, channel_multiplier=0, allow_small_or_imprecise_dtypes=True)
            nc.gpsimd.iota(iota_part[:, :], [[0, 1]], base=0, channel_multiplier=1, allow_small_or_imprecise_dtypes=True)
            nc.gpsimd.iota(iota_tile[:, :], [[1, TILES]], base=0, channel_multiplier=0,
                           allow_small_or_imprecise_dtypes=True).then_inc(s_iota, 1)

            chain = Chain(pool, s_pch)

            def settle(eng_copy):
                chain.link(eng_copy)
                nc.gpsimd.tensor_tensor(settled[:, :], iota_part[0:1, :], iota_part[0:1, :], ALU.add)

            def scatter(n, k):
                pool.wait_ge(s_slots, n + 1)
                pool.wait_ge(s_padrec, 32)
                with pool.Fori(0, SITERS) as i:
                    chain.enter(i, 2)
                    for h in (0, 1):
                        pool.wait_ge(s_scat[h], i * (16 * HALF) + n * SITERS * 16 * HALF)
                        j = i * (2 * HALF) + h * HALF
                        nc.gpsimd.tensor_copy(stage_slot[:, h, :], slot[k][:, bass.ds(j, HALF)])
                        settle(nc.gpsimd.tensor_copy(stage_rec[:, h, :, :], rec[k][:, bass.ds(j, HALF), :]))
                        for t in range(HALF):
                            nc.gpsimd.indirect_dma_start(
                                rec_dram[k], bass.IndirectOffsetOnAxis(ap=stage_slot[:, h, t:t + 1].bitcast(U32), axis=0),
                                stage_rec[:, h, t, :], None).then_inc(s_scat[h], 16)
                chain.leave(SITERS)

            def gather(name, key, free_sem, free_base, tables):
                g = GATHER.index(name)
                pool.wait_ge(s_sorted[key], 16)
                pool.wait_ge(s_table, 16 * NC * tables)
                with pool.Fori(0, ITERS) as i:
                    chain.enter(i, 2)
                    for h in (0, 1):
                        pool.wait_ge(free_sem, i * 2 + (free_base + h - 1))
                        settle(nc.gpsimd.tensor_copy(stage_idx[:, h, :],
                                                         slots[key][:, bass.ds(i * (2 * HALF) + h * HALF, HALF), 0]))
                        for t in range(HALF):
                            nc.gpsimd.indirect_dma_start(
                                rows[:, h, t, :], None, tab[name],
                                bass.IndirectOffsetOnAxis(ap=stage_idx[:, h, t:t + 1].bitcast(U32), axis=0)).then_inc(s_got[h], 16)
                chain.leave(ITERS)

            for n, k in enumerate(("dst", "src")):
                scatter(n, k)
            gather("msg", "dst", s_mixed, 1, 1)
            for l in range(LAYERS):
                gather(f"gru{l}", "dst", s_seg, STEPS * (l + 1), 2 + l)
            gather("sage", "dst", s_seg, STEPS * (LAYERS + 1), LAYERS + 2)
            gather("scores", "src", s_mixed, 1 + STEPS, LAYERS + 3)
            pool.wait_ge(s_mixed, 1 + 2 * STEPS)
            gather("values", "src", s_paid, STEPS, LAYERS + 4)

        @block.tensor
        def _(pe):
            mm = nc.tensor.matmul

            def start_dense(stage):
                if BASE[stage]:
                    pe.wait_ge(s_emptied, BASE[stage])

            def free(stage, c):
                if c >= 2:
                    pe.wait_ge(s_emptied, BASE[stage] + c - 1)

            def squares(stage, emit):
                start_dense(stage)
                for c, (w0, nw) in enumerate(CHUNKS):
                    free(stage, c)
                    for k in range(nw):
                        last = emit(bank(c % 2)[:, k * P:(k + 1) * P], w0 + k)
                    last.then_inc(s_filled, 1)

            def wide(stage, emit):
                start_dense(stage)
                for c, (w0, nw) in enumerate(CHUNKS):
                    free(stage, c)
                    emit(bank(c % 2, nw * P), slice(w0 * P, (w0 + nw) * P)).then_inc(s_filled, 1)

            def turn(src):
                return lambda o, w: nc.tensor.transpose(o, src[:, w, 0:D], ident[:, :])

            def of_window(lhs, rhs):
                return lambda o, w: mm(o, lhs[:, w * P:(w + 1) * P], rhs, start=True, stop=True)

            def segments(name, kind, hot_base, paid_base=None):
                g, sbase = GATHER.index(name), SEG.index(name) * STEPS
                with pe.Fori(0, ITERS) as i:
                    for h in (0, 1):
                        seg_step(name, kind, i, h, g, sbase, hot_base, paid_base)

            def seg_step(name, kind, i, h, g, sbase, hot_base, paid_base):
                pe.wait_ge(s_hot, i * 2 + (hot_base + h + 1))
                if kind == "T":
                    pe.wait_ge(s_got[h], i * (16 * HALF) + (g * ITERS + 1) * 16 * HALF)
                    pe.wait_ge(s_added, i * 2 + (sbase + h - 1))
                    o8 = eight(4 + 2 * h)
                    for k in range(HALF):
                        last = mm(o8[:, k, :], rows[:, h, k, :], onehot[:, h, k, :], start=True, stop=True)
                else:
                    pe.wait_ge(s_paid, i * 2 + (paid_base + h + 1))
                    pe.wait_ge(s_added, i * 2 + (sbase + h))
                    for k in range(HALF):
                        last = mm(seg_slot(k, kind), onehot[:, h, k, :], pay[:, h, k, 0:kind], start=True, stop=True)
                last.then_inc(s_seg, 1)

            def spread_step(name, key, i, h, hot_base):
                b = SPREAD.index(name) * STEPS
                wins = windows_of(PE, key, i, h)
                pe.wait_ge(s_hot, i * 2 + (hot_base + h + 1))
                pe.wait_ge(s_hotT, i * 2 + (b + h))
                o8 = eight(0)
                for k in range(HALF):
                    last = nc.tensor.transpose(o8[:, k, :], onehot[:, h, k, :], ident[:, :])
                last.then_inc(s_turned, 1)
                pe.wait_ge(s_hotT, i * 2 + (b + h + 1))
                pe.wait_ge(s_mixed, i * 2 + (b + h + 1))
                o8 = eight(2)
                for k in range(HALF):
                    last = mm(o8[:, k, :], onehotT[:, k, :], q_win[:, bass.ds(wins[k], 1), :].rearrange("p a d -> p (a d)"),
                              start=True, stop=True)
                last.then_inc(s_spread, 1)

            pe.wait_ge(s_stage, STAGE["consts"])
            for n in range(2):
                pe.wait_ge(s_binned, n + 1)
                if n:
                    pe.wait_ge(s_slots, n)
                mm(ps[0:EP, 7, 0:WINS], before[0:EP, 0:EP], cnt_p[:, :], start=True, stop=True)
                mm(ps[:, 7, 64:64 + WINS], ones[0:EP, :], cnt_p[:, :], start=True, stop=True).then_inc(s_totals, 1)

            pe.wait_ge(s_w, 16 * N_W)
            for c in range(3):
                free("turn_weights", c)
                for k in range(4):
                    last = nc.tensor.transpose(bank(c % 2)[:, k * P:(k + 1) * P], w_raw[:, 4 * c + k, :], ident[:, :])
                last.then_inc(s_filled, 1)
            free("turn_weights", 3)
            nc.tensor.transpose(ps[:, 1, 0:HEADS], we2_raw[:, :], ident[0:HEADS, 0:HEADS]).then_inc(s_filled, 1)

            pe.wait_ge(s_slots, 2)
            pe.wait_ge(s_x, 32)
            squares("x0T", turn(xn))
            squares("p_table", of_window(xT, w_m1[:, 0, :]))
            squares("q0", of_window(xT, w_m1[:, 1, :]))
            pe.wait_ge(s_emptied, BASE["q0"] + NC)
            with pe.Fori(0, ITERS) as i:
                for h in (0, 1):
                    spread_step("msg", "dst", i, h, 0)
                    seg_step("msg", D + 1, i, h, 0, 0, 0, 0)
            pe.wait_ge(s_added, STEPS)
            squares("H_T", turn(acc))
            start_dense("count_T")
            nc.tensor.transpose(ps[0:WINS, 0, 0:P], acc[:, :, D], ident[:, :]).then_inc(s_filled, 1)
            wide("agg0", lambda o, s: mm(o, w_m2[:, :], uT[:, s], start=True, stop=True))

            def u1(o, s):
                mm(o, w_u1[:, 0, :], xT[:, s], start=True, stop=False)
                return mm(o, w_u1[:, 1, :], aggT[:, s], start=False, stop=True)

            wide("u1", u1)
            squares("h2", of_window(uT, w_u2[:, :]))
            pe.wait_ge(s_stage, STAGE["x1"])
            squares("x1T", turn(xn))

            for l in range(LAYERS):
                squares(f"y{l}", of_window(xT, w_gg[:, l, :]))
                segments(f"gru{l}", "T", STEPS * (l + 1))
                pe.wait_ge(s_added, STEPS * (l + 2))
                start_dense(f"gru{l}")
                for c, (w0, nw) in enumerate(CHUNKS):
                    free(f"gru{l}", c)
                    s, b, m = slice(w0 * P, (w0 + nw) * P), 4 * (c % 2), nw * P
                    for g in (0, 1):
                        mm(bank(b + g, m), wT[:, g, :], aggT[:, s], start=True, stop=False)
                        mm(bank(b + g, m), wT[:, 3 + g, :], xT[:, s], start=False, stop=True)
                    mm(bank(b + 2, m), wT[:, 2, :], aggT[:, s], start=True, stop=True)
                    mm(bank(b + 3, m), wT[:, 5, :], xT[:, s], start=True, stop=True).then_inc(s_filled, 1)
            squares("h_back", lambda o, w: nc.tensor.transpose(o, xT[:, w * P:(w + 1) * P], ident[:, :]))
            pe.wait_ge(s_stage, STAGE["x2"])
            squares("x2T", turn(xn))

            segments("sage", "T", STEPS * (LAYERS + 1))
            pe.wait_ge(s_stage, STAGE["means"])

            def sage(o, w):
                mm(o, uT[:, w * P:(w + 1) * P], wT[:, 6, :], start=True, stop=False)
                return mm(o, xT[:, w * P:(w + 1) * P], wT[:, 7, :], start=False, stop=True)

            squares("sage", sage)
            pe.wait_ge(s_stage, STAGE["x3"])
            squares("x3T", turn(xn))

            squares("q3", of_window(xT, wT[:, 8, :]))
            squares("k3", of_window(xT, wT[:, 9, :]))
            squares("v3", of_window(xT, wT[:, 10, :]))
            with pe.Fori(0, ITERS) as i:
                for h in (0, 1):
                    pe.wait_ge(s_ebt, i * 2 + h)
                    pe.wait_ge(s_len, i * 2 + (h + 1))
                    nc.tensor.transpose(ps[0:HALF, 7, 0:P], stage_len[:, h, :], ident[:, :]).then_inc(s_lenT, 1)
                    pe.wait_ge(s_lenS, i * 2 + (h + 1))
                    pe.wait_ge(s_hid, i * 2 + h)
                    for k in range(HALF):
                        last = mm(eight(0)[:, k, :], we1_sel[:, k, :], lenT[:, h, :], start=True, stop=True)
                    last.then_inc(s_pre, 1)
                    pe.wait_ge(s_hid, i * 2 + (h + 1))
                    for k in range(HALF):
                        last = mm(ps[:, 6, k * HEADS:(k + 1) * HEADS], hidT[:, k, :], we2T[:, :], start=True, stop=True)
                    last.then_inc(s_eb, 1)
            hot3 = STEPS * (LAYERS + 2)
            with pe.Fori(0, ITERS) as i:
                for h in (0, 1):
                    spread_step("scores", "src", i, h, hot3)
            pe.wait_ge(s_stage, STAGE["scored"])
            nc.tensor.transpose(ps[0:HEADS, 0, 0:P], hmax[:, :], ident[:, :]).then_inc(s_filled, 1)
            pe.wait_ge(s_stage, STAGE["max_diag"])
            mm(ps[:, 0, 0:HEADS], ones[0:HEADS, :], hdiag[:, :], start=True, stop=True).then_inc(s_filled, 1)
            segments("values", PAY, hot3 + STEPS, STEPS)
            pe.wait_ge(s_stage, STAGE["out_norm"])
            squares("o_T", turn(acc))
            squares("o_out", of_window(uT, wT[:, 11, :]))

        @block.scalar
        def _(act):
            chain = Chain(act, s_ach)

            def empty(stage, emit):
                for c, (w0, nw) in enumerate(CHUNKS):
                    act.wait_ge(s_filled, BASE[stage] + c + 1)
                    emit(bank(c % 2, nw * P), w0, nw).then_inc(s_emptied, 1)

            def flat(dst):
                return lambda o, w0, nw: nc.scalar.copy(dst[:, w0 * P:(w0 + nw) * P], o)

            def rows_to(dst):
                return lambda o, w0, nw: nc.scalar.copy(dst[:, w0:w0 + nw, :].rearrange("p w d -> p (w d)"), o)

            def root(n):
                act.wait_ge(s_norm, n + 1)
                nc.scalar.activation(std[:, :], mv[:, :, 1], ACT.Sqrt, bias=eps_col[:, 0:1]).then_inc(s_std, 1)

            def copy_turned(b, i, h):
                act.wait_ge(s_turned, i * 2 + (b + h + 1))
                act.wait_ge(s_spread, i * 2 + (b + h))
                nc.scalar.copy(onehotT[:, :, :].rearrange("p k n -> p (k n)"),
                               ps[:, 0:2, :].rearrange("p b c -> p (b c)")).then_inc(s_hotT, 1)

            for c in range(3):
                act.wait_ge(s_filled, c + 1)
                nc.scalar.copy(wT[:, 4 * c:4 * c + 4, :].rearrange("p w d -> p (w d)"), bank(c % 2)).then_inc(s_emptied, 1)
            act.wait_ge(s_filled, 4)
            nc.scalar.copy(we2T[:, :], ps[:, 1, 0:HEADS]).then_inc(s_emptied, 1)

            empty("x0T", flat(xT))
            empty("p_table", rows_to(big))
            with act.Fori(0, ITERS) as i:
                for h in (0, 1):
                    copy_turned(0, i, h)
                    act.wait_ge(s_mixed, i * 2 + (h + 2))
                    nc.scalar.activation(pay[:, h, :, 0:D], pay[:, h, :, 0:D], ACT.Relu).then_inc(s_paid, 1)
            empty("H_T", flat(uT))
            act.wait_ge(s_filled, BASE["count_T"] + 1)
            nc.scalar.copy(countT[:, :], ps[0:WINS, 0, 0:P]).then_inc(s_emptied, 1)
            empty("u1", lambda o, w0, nw: nc.scalar.activation(uT[:, w0 * P:(w0 + nw) * P], o, ACT.Relu, bias=cols[:, 1:2]))
            root(0)
            root(1)
            empty("x1T", flat(xT))
            for l in range(LAYERS):
                empty(f"y{l}", rows_to(big))
                for c, (w0, nw) in enumerate(CHUNKS):
                    g, b, m = BASE[f"gru{l}"] + c, 4 * (c % 2), nw * P
                    act.wait_ge(s_filled, g + 1)
                    if c >= 2:
                        act.wait_ge(s_emptied, g - 1)
                    nc.scalar.activation(g_r[:, c % 2, 0:m], bank(b, m), ACT.Sigmoid, bias=b_rz[:, 0:1])
                    nc.scalar.activation(g_z[:, c % 2, 0:m], bank(b + 1, m), ACT.Sigmoid, bias=b_rz[:, 1:2]).then_inc(s_gates, 1)
                    act.wait_ge(s_cand, l * NC + c + 1)
                    nc.scalar.activation(g_n[:, c % 2, 0:m], g_n[:, c % 2, 0:m], ACT.Tanh, bias=cols[:, 4:5]).then_inc(s_tanh, 1)
            root(2)
            empty("x2T", flat(xT))
            root(3)
            empty("x3T", flat(xT))
            act.wait_ge(s_cutarg, 1)
            nc.scalar.activation(cut[:, :], tmp_t[:, :], ACT.Sin, bias=halfpi_col[:, 0:1], scale=-float(np.pi) / CUTOFF).then_inc(s_cut, 1)
            with act.Fori(0, ITERS) as i:
                for h in (0, 1):
                    nc.scalar.copy(stage_len[:, h, :], slots["src"][:, bass.ds(i * (2 * HALF) + h * HALF, HALF), 2].bitcast(F32)).then_inc(s_len, 1)
                    act.wait_ge(s_lenT, i * 2 + (h + 1))
                    nc.scalar.copy(lenT[:, h, :], ps[0:HALF, 7, 0:P]).then_inc(s_lenS, 1)
                    act.wait_ge(s_pre, i * 2 + (h + 1))
                    act.wait_ge(s_eb, i * 2 + h)
                    nc.scalar.activation(hidT[:, :, :].rearrange("p k n -> p (k n)"),
                                         ps[:, 0:2, :].rearrange("p b c -> p (b c)"),
                                         ACT.Silu, bias=cols[:, 8:9]).then_inc(s_hid, 1)
            with act.Fori(0, ITERS) as i:
                for h in (0, 1):
                    copy_turned(STEPS, i, h)
            act.wait_ge(s_stage, STAGE["exp_arg"])
            nc.scalar.activation(score[:, :, :], score[:, :, :], ACT.Exp).then_inc(s_exp, 1)
            empty("o_T", flat(uT))
            root(4)
            root(5)

        @block.vector
        def _(dve):
            chain = Chain(dve, s_dch)
            link = chain.link
            V = nc.vector
            norms = [0]

            def empty(stage, emit):
                for c, (w0, nw) in enumerate(CHUNKS):
                    dve.wait_ge(s_filled, BASE[stage] + c + 1)
                    emit(bank(c % 2, nw * P).rearrange("p (w d) -> p w d", d=D), w0, nw).then_inc(s_emptied, 1)

            def layer_norm(z, done=None):
                for w in range(WINS):
                    last = V.bn_stats(bn[:, w, :], z[:, w, :])
                link(last)
                for w in range(WINS):
                    last = V.bn_aggr(mv[:, w, :], bn[:, w, :])
                last.then_inc(s_norm, 1)
                norms[0] += 1
                dve.wait_ge(s_std, norms[0])
                link(V.reciprocal(std[:, :], std[:, :]))
                link(V.tensor_tensor(z[:, :, :], z[:, :, :], mv[:, :, 0:1].broadcast_to([P, WINS, D]), ALU.subtract))
                last = V.tensor_tensor(z[:, :, :], z[:, :, :], std[:, :].unsqueeze(2).broadcast_to([P, WINS, D]), ALU.mult)
                if done is None:
                    link(last)
                else:
                    last.then_inc(s_stage, 1)
                    dve.wait_ge(s_stage, done)

            def place(n, key, other):
                k_i, o_i, r, sl = edge_in[key], edge_in[other], rec[key], slot[key]
                link(V.tensor_scalar(word[:, :], k_i[:, :], 7, None, ALU.arith_shift_right))
                link(V.tensor_copy(win_f[:, :], word[:, :]))
                link(V.tensor_scalar(word[:, :], k_i[:, :], P - 1, None, ALU.bitwise_and))
                V.tensor_copy(r[:, :, 1].bitcast(F32), word[:, :])
                V.tensor_copy(r[:, :, 0], o_i[:, :])
                V.tensor_copy(r[:, :, 2], len_in[:, :].bitcast(I32))
                link(V.tensor_copy(r[:, :, 3], o_i[:, :]))
                for b in range(WINS):
                    last = V.tensor_scalar(hot[:, b, :], win_f[:, :], float(b), None, ALU.is_equal)
                link(last)
                h2 = arena[0][0:EP, :]
                link(V.tensor_tensor_scan(arena[1][0:EP, :], h2, h2, 0.0, ALU.add, ALU.max))
                V.memset(ends[:, 0:1], 0.0)
                link(V.tensor_copy(ends[:, 1:WINS + 1], rank[:, :, EJ - 1]))
                if n:
                    dve.wait_ge(s_totals, n)
                V.tensor_tensor(cnt_p[:, :], ends[:, 1:WINS + 1], ends[:, 0:WINS], ALU.subtract).then_inc(s_binned, 1)
                dve.wait_ge(s_totals, n + 1)
                link(V.tensor_scalar(need[:, :], ps[:, 7, 64:64 + WINS], float(P - 1), None, ALU.add))
                link(V.tensor_copy(need_i[:, :], need[:, :]))
                link(V.tensor_scalar(need_i[:, :], need_i[:, :], 7, None, ALU.arith_shift_right))
                link(V.tensor_copy(need[:, :], need_i[:, :]))
                link(V.tensor_tensor_scan(incl[:, :], need[:, :], need[:, :], 0.0, ALU.add, ALU.max))
                link(V.tensor_tensor(offs[:, :], incl[:, :], need[:, :], ALU.subtract))
                link(V.tensor_scalar(offs[:, :], offs[:, :], float(P), -1.0, ALU.mult, ALU.add))
                link(V.tensor_tensor(offs[0:EP, :], offs[0:EP, :], ends[:, 0:WINS], ALU.subtract))
                link(V.tensor_tensor(offs[0:EP, :], offs[0:EP, :], ps[0:EP, 7, 0:WINS], ALU.add))
                for b in range(WINS):
                    last = V.scalar_tensor_tensor(rank[:, b, :], rank[:, b, :], offs[0:EP, b:b + 1], hot[:, b, :], ALU.add, ALU.mult)
                link(last)
                link(V.tensor_reduce(win_f[:, :], rank[:, :, :].rearrange("p b j -> p j b"), AX.X, ALU.add))
                link(V.tensor_copy(word[:, :], win_f[:, :]))
                V.tensor_scalar(sl[:, :], word[:, :], P - 1, None, ALU.bitwise_and)
                link(V.tensor_scalar(slot_hi[:, :], word[:, :], 7, None, ALU.arith_shift_right))
                link(V.scalar_tensor_tensor(sl[:, :], sl[:, :], float(TILES), slot_hi[:, :], ALU.mult, ALU.add))
                tc = tile_cmp[:, 0:TILES * 24].rearrange("p (t b) -> p t b", b=24)
                link(V.tensor_tensor(tc, iota_tile[:, :].unsqueeze(2).broadcast_to([1, TILES, 24]),
                                     incl[0:1, 0:24].unsqueeze(1).broadcast_to([1, TILES, 24]), ALU.is_ge))
                link(V.tensor_reduce(tile_win_f[:, :], tc, AX.X, ALU.add))
                V.tensor_copy(tile_win[key][:, :], tile_win_f[:, :]).then_inc(s_slots, 1)

            def make_onehot(key, h, i):
                loc = slots[key][:, bass.ds(i * (2 * HALF) + h * HALF, HALF), 1:2].bitcast(F32)
                V.tensor_tensor(onehot[:, h, :, :], iota_free[:, :].unsqueeze(1).broadcast_to([P, HALF, P]),
                                loc.broadcast_to([P, HALF, P]), ALU.is_equal).then_inc(s_hot, 1)

            def add_up(key, i, h, sbase, source, dst):
                wins = windows_of(DVE, key, i, h)
                dve.wait_ge(s_seg, i * 2 + (sbase + h + 1))
                for k in range(HALF):
                    o = dst[:, bass.ds(wins[k], 1), :].rearrange("p a d -> p (a d)")
                    ins = V.tensor_tensor(o, o, source(k), ALU.add)
                    if k < HALF - 1:
                        link(ins)
                ins.then_inc(s_added, 1)

            V.memset(xn[:, WINS - 1, :], 0.0).then_inc(s_zero, 1)
            V.memset(ones[:, :], 1.0)
            V.memset(eps_col[:, :], EPS).then_inc(s_mixed, 1)
            V.memset(halfpi_col[:, :], float(np.pi) / 2)
            for k in ("dst", "src"):
                link(V.memset(slots[k][:, :, :], 0))
                link(V.memset(slots[k][:, :, 1].bitcast(F32), -1.0))
            V.memset(pay[:, :, :, :], 1.0).then_inc(s_padfill, 1)
            dve.wait_ge(s_iota, 1)
            V.tensor_scalar(before[:, :], iota_free[:, :], iota_part[:, 0:1], None, ALU.is_gt)
            V.tensor_scalar(ident[:, :], iota_free[:, :], iota_part[:, 0:1], None, ALU.is_equal).then_inc(s_stage, 1)

            dve.wait_ge(s_edges, 48)
            place(0, "dst", "src")
            dve.wait_ge(s_slots, 1)
            place(1, "src", "dst")
            dve.wait_ge(s_slots, 2)
            link(V.memset(acc[:, :, :], 0.0))

            dve.wait_ge(s_w, 16 * N_W)
            dve.wait_ge(s_stage, STAGE["consts"])
            V.tensor_tensor(b_rz[:, :], cols[:, 2:4], cols[:, 5:7], ALU.add)
            link(V.tensor_tensor(we1_sel[:, :, :], we1_row[:, :].unsqueeze(1).broadcast_to([HALF, HALF, P]),
                                 ident[0:HALF, 0:HALF].unsqueeze(2).broadcast_to([HALF, HALF, P]), ALU.mult))

            empty("q0", lambda o, w0, nw: V.tensor_tensor(q_win[:, w0:w0 + nw, :], o, vec("L0_gnn_b_m1", nw), ALU.add))
            dve.wait_ge(s_sorted["dst"], 16)
            with dve.Fori(0, ITERS) as i:
                chain.enter(i, 2 * (HALF - 1))
                for h in (0, 1):
                    make_onehot("dst", h, i)
                    dve.wait_ge(s_got[h], i * (16 * HALF) + 16 * HALF)
                    dve.wait_ge(s_spread, i * 2 + (h + 1))
                    V.tensor_tensor(pay[:, h, :, 0:D], rows[:, h, :, :], eight(2), ALU.add).then_inc(s_mixed, 1)
                    add_up("dst", i, h, 0, lambda k: seg_slot(k, D + 1), acc[:, :, 0:D + 1])
                chain.leave(ITERS)
            dve.wait_ge(s_added, STEPS)
            dve.wait_ge(s_count, 32)
            for c, (w0, nw) in enumerate(CHUNKS):
                s = slice(w0 * P, (w0 + nw) * P)
                dve.wait_ge(s_filled, BASE["agg0"] + c + 1)
                V.scalar_tensor_tensor(aggT[:, s], count_b[:, s], cols[:, 0:1], bank(c % 2, nw * P),
                                       ALU.mult, ALU.add).then_inc(s_emptied, 1)
            empty("h2", lambda o, w0, nw: V.tensor_tensor(big[:, w0:w0 + nw, :], o, vec("L0_gnn_b_u2", nw), ALU.add))
            dve.wait_ge(s_emptied, BASE["h2"] + NC)
            layer_norm(big)
            link(V.tensor_tensor(big[:, :, :], big[:, :, :], vec("L0_gnn_gamma", WINS), ALU.mult))
            link(V.tensor_tensor(big[:, :, :], big[:, :, :], vec("L0_gnn_beta", WINS), ALU.add))
            link(V.scalar_tensor_tensor(xn[:, :, :], xn[:, :, :], 2.0, big[:, :, :], ALU.mult, ALU.add))
            layer_norm(xn, STAGE["x1"])

            for l in range(LAYERS):
                if l == 0:
                    link(V.memset(aggT, 0.0))
                else:
                    dve.wait_ge(s_emptied, BASE[f"gru{l - 1}"] + NC)
                    link(V.memset(aggT, 0.0))
                with dve.Fori(0, ITERS) as i:
                    chain.enter(i, 2 * (HALF - 1))
                    for h in (0, 1):
                        make_onehot("dst", h, i)
                        add_up("dst", i, h, STEPS * (l + 1), lambda k: eight(4 + 2 * h)[:, k, :], aggT_w)
                    chain.leave(ITERS)
                for c, (w0, nw) in enumerate(CHUNKS):
                    s, b, m, g = slice(w0 * P, (w0 + nw) * P), 4 * (c % 2), nw * P, l * NC + c
                    r, z, n = (t[:, c % 2, 0:m] for t in (g_r, g_z, g_n))
                    dve.wait_ge(s_gates, g + 1)
                    link(V.scalar_tensor_tensor(n, bank(b + 3, m), cols[:, 7:8], r, ALU.add, ALU.mult))
                    V.tensor_tensor(n, n, bank(b + 2, m), ALU.add).then_inc(s_cand, 1)
                    dve.wait_ge(s_tanh, g + 1)
                    link(V.tensor_tensor(r, xT[:, s], n, ALU.subtract))
                    link(V.tensor_tensor(r, r, z, ALU.mult))
                    V.tensor_tensor(xT[:, s], r, n, ALU.add).then_inc(s_emptied, 1)
            empty("h_back", lambda o, w0, nw: V.scalar_tensor_tensor(
                xn[:, w0:w0 + nw, :].rearrange("p w d -> p (w d)"), xn[:, w0:w0 + nw, :].rearrange("p w d -> p (w d)"), 2.0,
                o.rearrange("p w d -> p (w d)"), ALU.mult, ALU.add))
            dve.wait_ge(s_emptied, BASE["h_back"] + NC)
            layer_norm(xn, STAGE["x2"])

            link(V.memset(aggT, 0.0))
            with dve.Fori(0, ITERS) as i:
                chain.enter(i, 2 * (HALF - 1))
                for h in (0, 1):
                    make_onehot("dst", h, i)
                    add_up("dst", i, h, STEPS * (LAYERS + 1), lambda k: eight(4 + 2 * h)[:, k, :], aggT_w)
                chain.leave(ITERS)
            dve.wait_ge(s_added, STEPS * (LAYERS + 2))
            link(V.tensor_scalar(count_b[:, :], count_b[:, :], 1.0, None, ALU.max))
            link(V.reciprocal(count_b[:, :], count_b[:, :]))
            V.tensor_tensor(uT[:, :], aggT, count_b[:, :], ALU.mult).then_inc(s_stage, 1)
            empty("sage", lambda o, w0, nw: V.tensor_tensor(big[:, w0:w0 + nw, :], o, vec("L2_gnn_b", nw), ALU.add))
            dve.wait_ge(s_emptied, BASE["sage"] + NC)
            dve.wait_ge(s_table, 16 * NC * (LAYERS + 2))
            link(V.scalar_tensor_tensor(xn[:, :, :], big[:, :, :], 0.0, xn[:, :, :], ALU.max, ALU.add))
            layer_norm(xn, STAGE["x3"])

            dve.wait_ge(s_sorted["src"], 16)
            empty("q3", lambda o, w0, nw: V.tensor_tensor(q_win[:, w0:w0 + nw, :], o, vec("L3_gnn_bq", nw), ALU.add))
            empty("k3", lambda o, w0, nw: V.tensor_tensor(big[:, w0:w0 + nw, :], o, vec("L3_gnn_bk", nw), ALU.add))
            dve.wait_ge(s_table, 16 * NC * (LAYERS + 3))
            empty("v3", lambda o, w0, nw: V.tensor_tensor(big[:, w0:w0 + nw, :], o, vec("L3_gnn_bv", nw), ALU.add))
            length = slots["src"][:, :, 2].bitcast(F32)
            link(V.tensor_scalar(live[:, :], slots["src"][:, :, 1].bitcast(F32), 0.0, None, ALU.is_ge))
            link(V.tensor_scalar(tmp_t[:, :], length, 1.0 / (2 * CUTOFF), ROUND, ALU.mult, ALU.add))
            link(V.tensor_scalar(tmp_t[:, :], tmp_t[:, :], -ROUND, None, ALU.add))
            link(V.scalar_tensor_tensor(tmp_t[:, :], tmp_t[:, :], -2 * CUTOFF, length, ALU.mult, ALU.add))
            link(V.tensor_scalar(cut[:, :], tmp_t[:, :], -1.0, None, ALU.mult))
            V.tensor_tensor(tmp_t[:, :], tmp_t[:, :], cut[:, :], ALU.max).then_inc(s_cutarg, 1)
            dve.wait_ge(s_cut, 1)
            link(V.tensor_scalar(cut[:, :], cut[:, :], 1.0, 0.5, ALU.add, ALU.mult))
            link(V.scalar_tensor_tensor(cut[:, :], length, CUTOFF, cut[:, :], ALU.is_lt, ALU.mult))
            with dve.Fori(0, ITERS) as i:
                for h in (0, 1):
                    dve.wait_ge(s_eb, i * 2 + (h + 1))
                    V.tensor_tensor(bias_e[:, bass.ds(i * (2 * HALF) + h * HALF, HALF), :],
                                    ps[:, 6, 0:HALF * HEADS].rearrange("p (k h) -> p k h", h=HEADS),
                                    be2[:, :].unsqueeze(1).broadcast_to([P, HALF, HEADS]), ALU.add).then_inc(s_ebt, 1)
            with dve.Fori(0, ITERS) as i:
                chain.enter(i, 2)
                for h in (0, 1):
                    g = GATHER.index("scores")
                    make_onehot("src", h, i)
                    dve.wait_ge(s_got[h], i * (16 * HALF) + (g * ITERS + 1) * 16 * HALF)
                    dve.wait_ge(s_spread, i * 2 + (STEPS + h + 1))
                    link(V.tensor_tensor(pay[:, h, :, 0:D], rows[:, h, :, :], eight(2), ALU.mult))
                    V.tensor_reduce(score[:, bass.ds(i * (2 * HALF) + h * HALF, HALF), :],
                                    pay[:, h, :, 0:D].rearrange("p k (h d) -> p k h d", d=HD), AX.X, ALU.add).then_inc(s_mixed, 1)
                chain.leave(ITERS)
            dve.wait_ge(s_mixed, 1 + 2 * STEPS)
            dve.wait_ge(s_ebt, STEPS)
            cut_b = cut[:, :].unsqueeze(2).broadcast_to([P, TILES, HEADS])
            live_b = live[:, :].unsqueeze(2).broadcast_to([P, TILES, HEADS])
            link(V.scalar_tensor_tensor(score[:, :, :], score[:, :, :], float(HD) ** -0.5, bias_e[:, :, :], ALU.mult, ALU.add))
            link(V.tensor_tensor(score[:, :, :], score[:, :, :], cut_b, ALU.mult))
            link(V.tensor_tensor(score[:, :, :], score[:, :, :], live_b, ALU.mult))
            link(V.tensor_scalar(live[:, :], live[:, :], -1.0, 1e30, ALU.add, ALU.mult))
            link(V.tensor_tensor(score[:, :, :], score[:, :, :], live_b, ALU.add))
            V.tensor_reduce(hmax[:, :], score[:, :, :].rearrange("p t h -> p h t"), AX.X, ALU.max).then_inc(s_stage, 1)
            dve.wait_ge(s_filled, BASE["max_T"] + 1)
            V.tensor_reduce(hmaxT[:, :], ps[0:HEADS, 0, 0:P], AX.X, ALU.max).then_inc(s_emptied, 1)
            dve.wait_ge(s_emptied, BASE["max_T"] + 1)
            V.tensor_scalar(hdiag[:, :], ident[0:HEADS, 0:HEADS], hmaxT[:, 0:1], None, ALU.mult).then_inc(s_stage, 1)
            dve.wait_ge(s_filled, BASE["max_back"] + 1)
            V.tensor_copy(hmax_b[:, :], ps[:, 0, 0:HEADS]).then_inc(s_emptied, 1)
            dve.wait_ge(s_emptied, BASE["max_back"] + 1)
            V.tensor_tensor(score[:, :, :], score[:, :, :], hmax_b[:, :].unsqueeze(1).broadcast_to([P, TILES, HEADS]),
                            ALU.subtract).then_inc(s_stage, 1)
            link(V.memset(acc[:, :, :], 0.0))
            dve.wait_ge(s_exp, 1)
            with dve.Fori(0, ITERS) as i:
                chain.enter(i, 2 * (HALF - 1))
                for h in (0, 1):
                    g = GATHER.index("values")
                    p8 = score[:, bass.ds(i * (2 * HALF) + h * HALF, HALF), :]
                    make_onehot("src", h, i)
                    dve.wait_ge(s_got[h], i * (16 * HALF) + (g * ITERS + 1) * 16 * HALF)
                    V.tensor_copy(pay[:, h, :, D:PAY], p8)
                    V.tensor_tensor(pay[:, h, :, 0:D].rearrange("p k (h d) -> p k h d", d=HD),
                                    rows[:, h, :, :].rearrange("p k (h d) -> p k h d", d=HD),
                                    p8.unsqueeze(3).broadcast_to([P, HALF, HEADS, HD]), ALU.mult).then_inc(s_paid, 1)
                    add_up("src", i, h, STEPS * (LAYERS + 2), lambda k: seg_slot(k, PAY), acc[:, :, :])
                chain.leave(ITERS)
            dve.wait_ge(s_added, STEPS * (LAYERS + 3))
            link(V.tensor_scalar(den[:, :, :], acc[:, :, D:PAY], 1e-8, None, ALU.add))
            link(V.reciprocal(den[:, :, :], den[:, :, :]))
            V.tensor_tensor(acc[:, :, 0:D].rearrange("p w (h d) -> p w h d", d=HD),
                            acc[:, :, 0:D].rearrange("p w (h d) -> p w h d", d=HD),
                            den[:, :, :].unsqueeze(3).broadcast_to([P, WINS, HEADS, HD]), ALU.mult).then_inc(s_stage, 1)
            empty("o_out", lambda o, w0, nw: V.tensor_tensor(big[:, w0:w0 + nw, :], o, vec("L3_gnn_bo", nw), ALU.add))
            dve.wait_ge(s_emptied, BASE["o_out"] + NC)
            link(V.tensor_tensor(big[:, :, :], big[:, :, :], xn[:, :, :], ALU.add))
            layer_norm(big)
            link(V.tensor_tensor(big[:, :, :], big[:, :, :], vec("L3_gnn_ln_g", WINS), ALU.mult))
            link(V.tensor_tensor(big[:, :, :], big[:, :, :], vec("L3_gnn_ln_b", WINS), ALU.add))
            link(V.tensor_tensor(xn[:, :, :], xn[:, :, :], big[:, :, :], ALU.add))
            layer_norm(xn, STAGE["done"])


_INS = ["x", "src", "dst", "edge_weight1", "L0_gnn_w_m1", "L0_gnn_b_m1", "L0_gnn_w_m2", "L0_gnn_b_m2", "L0_gnn_w_u1",
        "L0_gnn_b_u1", "L0_gnn_w_u2", "L0_gnn_b_u2", "L0_gnn_gamma", "L0_gnn_beta", "L1_gnn_weight", "L1_gnn_w_ih",
        "L1_gnn_w_hh", "L1_gnn_b_ih", "L1_gnn_b_hh", "L2_gnn_W_l", "L2_gnn_W_r", "L2_gnn_b", "L3_gnn_Wq", "L3_gnn_bq",
        "L3_gnn_Wk", "L3_gnn_bk", "L3_gnn_Wv", "L3_gnn_bv", "L3_gnn_We1", "L3_gnn_be1", "L3_gnn_We2", "L3_gnn_be2",
        "L3_gnn_Wo", "L3_gnn_bo", "L3_gnn_ln_g", "L3_gnn_ln_b"]


def kernel(**inputs):
    import concourse.bacc as bacc
    from concourse.bass_utils import run_bass_kernel_spmd

    nc = bacc.Bacc("TRN2", target_bir_lowering=False, num_devices=1)
    arrays, aps = {}, {}
    for name in _INS:
        arr = np.ascontiguousarray(inputs[name])
        arrays[f"in_{name}"] = arr
        aps[name] = nc.dram_tensor(f"in_{name}", arr.shape, mybir.dt.from_np(arr.dtype), kind="ExternalInput").ap()
    out = nc.dram_tensor("out", (N, D), F32, kind="ExternalOutput").ap()
    gnn_program(nc, aps, out)
    r = run_bass_kernel_spmd(nc, [arrays], core_ids=[0])
    return r.results[0]["out"]
```
